# Optimizing a Trainium2 kernel written in Bass

```python
import numpy as np
import jax
import jax.numpy as jnp

def _softmax(x, axis=-1):
    return jax.nn.softmax(x, axis=axis)

def _gelu(x):
    return jax.nn.gelu(x, approximate=True)

def _silu(x):
    return jax.nn.silu(x)

def _sigmoid(x):
    return jax.nn.sigmoid(x)

def _layernorm(x, axis=-1, eps=1e-05):
    m = jnp.mean(x, axis=axis, keepdims=True)
    v = jnp.var(x, axis=axis, keepdims=True)
    return (x - m) / jnp.sqrt(v + eps)

def _scatter_add(tgt, idx, src, axis=0):
    return tgt.at[idx].add(src)

def _segment_sum(src, seg, n):
    return jax.ops.segment_sum(src, seg, n)
kernel_name = 'mk_dlrm_tower_d1_rec_r8_eba706'

def setup_inputs(seed: int=0):
    np.random.seed(seed)
    _w = jnp.asarray

    def _rec_inputs():
        import jax
        import jax.numpy as jnp
        _tk = jax.random.key(seed)
        dense_ctx = jax.random.normal(jax.random.fold_in(_tk, 190), (512, 16), jnp.float32)
        ids = jnp.stack([jax.random.randint(jax.random.fold_in(_tk, 200 + f), (512,), 0, v, jnp.int32) for f, v in enumerate([1250, 12500, 1000, 12500, 125000, 1000, 1000, 1250, 1000, 12500, 12500, 1250, 12500, 1000, 12500, 12500, 12500, 1000, 12500, 1000, 1000, 1250, 1000, 1000, 1000, 1000, 1000])], axis=1)
        tbl_0 = 0.05 * jax.random.normal(jax.random.fold_in(_tk, 500 + 0), (1250, 128), jnp.float32)
        tbl_1 = 0.05 * jax.random.normal(jax.random.fold_in(_tk, 500 + 1), (12500, 128), jnp.float32)
        tbl_2 = 0.05 * jax.random.normal(jax.random.fold_in(_tk, 500 + 2), (1000, 128), jnp.float32)
        tbl_3 = 0.05 * jax.random.normal(jax.random.fold_in(_tk, 500 + 3), (12500, 128), jnp.float32)
        tbl_4 = 0.05 * jax.random.normal(jax.random.fold_in(_tk, 500 + 4), (125000, 128), jnp.float32)
        tbl_5 = 0.05 * jax.random.normal(jax.random.fold_in(_tk, 500 + 5), (1000, 128), jnp.float32)
        tbl_6 = 0.05 * jax.random.normal(jax.random.fold_in(_tk, 500 + 6), (1000, 128), jnp.float32)
        tbl_7 = 0.05 * jax.random.normal(jax.random.fold_in(_tk, 500 + 7), (1250, 128), jnp.float32)
        tbl_8 = 0.05 * jax.random.normal(jax.random.fold_in(_tk, 500 + 8), (1000, 128), jnp.float32)
        tbl_9 = 0.05 * jax.random.normal(jax.random.fold_in(_tk, 500 + 9), (12500, 128), jnp.float32)
        tbl_10 = 0.05 * jax.random.normal(jax.random.fold_in(_tk, 500 + 10), (12500, 128), jnp.float32)
        tbl_11 = 0.05 * jax.random.normal(jax.random.fold_in(_tk, 500 + 11), (1250, 128), jnp.float32)
        tbl_12 = 0.05 * jax.random.normal(jax.random.fold_in(_tk, 500 + 12), (12500, 128), jnp.float32)
        tbl_13 = 0.05 * jax.random.normal(jax.random.fold_in(_tk, 500 + 13), (1000, 128), jnp.float32)
        tbl_14 = 0.05 * jax.random.normal(jax.random.fold_in(_tk, 500 + 14), (12500, 128), jnp.float32)
        tbl_15 = 0.05 * jax.random.normal(jax.random.fold_in(_tk, 500 + 15), (12500, 128), jnp.float32)
        tbl_16 = 0.05 * jax.random.normal(jax.random.fold_in(_tk, 500 + 16), (12500, 128), jnp.float32)
        tbl_17 = 0.05 * jax.random.normal(jax.random.fold_in(_tk, 500 + 17), (1000, 128), jnp.float32)
        tbl_18 = 0.05 * jax.random.normal(jax.random.fold_in(_tk, 500 + 18), (12500, 128), jnp.float32)
        tbl_19 = 0.05 * jax.random.normal(jax.random.fold_in(_tk, 500 + 19), (1000, 128), jnp.float32)
        tbl_20 = 0.05 * jax.random.normal(jax.random.fold_in(_tk, 500 + 20), (1000, 128), jnp.float32)
        tbl_21 = 0.05 * jax.random.normal(jax.random.fold_in(_tk, 500 + 21), (1250, 128), jnp.float32)
        tbl_22 = 0.05 * jax.random.normal(jax.random.fold_in(_tk, 500 + 22), (1000, 128), jnp.float32)
        tbl_23 = 0.05 * jax.random.normal(jax.random.fold_in(_tk, 500 + 23), (1000, 128), jnp.float32)
        tbl_24 = 0.05 * jax.random.normal(jax.random.fold_in(_tk, 500 + 24), (1000, 128), jnp.float32)
        tbl_25 = 0.05 * jax.random.normal(jax.random.fold_in(_tk, 500 + 25), (1000, 128), jnp.float32)
        tbl_26 = 0.05 * jax.random.normal(jax.random.fold_in(_tk, 500 + 26), (1000, 128), jnp.float32)
        _rk = jax.random.fold_in(_tk, 7)
        W_top1 = 0.0521996 * jax.random.normal(jax.random.fold_in(_tk, 801), (367, 512), jnp.float32)
        W_top2 = 0.0441942 * jax.random.normal(jax.random.fold_in(_tk, 802), (512, 256), jnp.float32)
        W_top3 = 0.0625 * jax.random.normal(jax.random.fold_in(_tk, 803), (256, 1), jnp.float32)
        b_top1 = jnp.zeros((512,), jnp.float32)
        b_top2 = jnp.zeros((256,), jnp.float32)
        return (dense_ctx, ids, tbl_0, tbl_1, tbl_2, tbl_3, tbl_4, tbl_5, tbl_6, tbl_7, tbl_8, tbl_9, tbl_10, tbl_11, tbl_12, tbl_13, tbl_14, tbl_15, tbl_16, tbl_17, tbl_18, tbl_19, tbl_20, tbl_21, tbl_22, tbl_23, tbl_24, tbl_25, tbl_26, W_top1, b_top1, W_top2, b_top2, W_top3)
    dense_ctx, ids, tbl_0, tbl_1, tbl_2, tbl_3, tbl_4, tbl_5, tbl_6, tbl_7, tbl_8, tbl_9, tbl_10, tbl_11, tbl_12, tbl_13, tbl_14, tbl_15, tbl_16, tbl_17, tbl_18, tbl_19, tbl_20, tbl_21, tbl_22, tbl_23, tbl_24, tbl_25, tbl_26, W_top1, b_top1, W_top2, b_top2, W_top3 = _rec_inputs()

    def _L0_rec_setup():
        import jax, jax.numpy as jnp
        import numpy as np
        key = jax.random.key(seed)
        B, F, D = (2048, 27, 128)
        inputs = jax.random.normal(key, (B, F, D), dtype=jnp.float32)
        return {'inputs': inputs, 'num_feas': F}
    _L0_rec_all = _L0_rec_setup()
    _L0_rec_in = {k: v for k, v in _L0_rec_all.items() if k in ()}
    del _L0_rec_all
    return {'dense_ctx': dense_ctx, 'ids': ids, 'tbl_0': tbl_0, 'tbl_1': tbl_1, 'tbl_2': tbl_2, 'tbl_3': tbl_3, 'tbl_4': tbl_4, 'tbl_5': tbl_5, 'tbl_6': tbl_6, 'tbl_7': tbl_7, 'tbl_8': tbl_8, 'tbl_9': tbl_9, 'tbl_10': tbl_10, 'tbl_11': tbl_11, 'tbl_12': tbl_12, 'tbl_13': tbl_13, 'tbl_14': tbl_14, 'tbl_15': tbl_15, 'tbl_16': tbl_16, 'tbl_17': tbl_17, 'tbl_18': tbl_18, 'tbl_19': tbl_19, 'tbl_20': tbl_20, 'tbl_21': tbl_21, 'tbl_22': tbl_22, 'tbl_23': tbl_23, 'tbl_24': tbl_24, 'tbl_25': tbl_25, 'tbl_26': tbl_26, 'W_top1': W_top1, 'b_top1': b_top1, 'W_top2': W_top2, 'b_top2': b_top2, 'W_top3': W_top3}

def reference(dense_ctx, ids, tbl_0, tbl_1, tbl_2, tbl_3, tbl_4, tbl_5, tbl_6, tbl_7, tbl_8, tbl_9, tbl_10, tbl_11, tbl_12, tbl_13, tbl_14, tbl_15, tbl_16, tbl_17, tbl_18, tbl_19, tbl_20, tbl_21, tbl_22, tbl_23, tbl_24, tbl_25, tbl_26, W_top1, b_top1, W_top2, b_top2, W_top3):
    import jax
    import jax.numpy as jnp

    def _L0_rec_ref(inputs, num_feas):
        import jax, jax.numpy as jnp
        import numpy as np
        dot_products = jnp.einsum('bnd,bmd->bnm', inputs, inputs)
        r, c = np.tril_indices(num_feas, k=-1)
        flat_interactions = dot_products[:, c, r]
        return flat_interactions
    e = jnp.stack([tbl_0[ids[:, 0]], tbl_1[ids[:, 1]], tbl_2[ids[:, 2]], tbl_3[ids[:, 3]], tbl_4[ids[:, 4]], tbl_5[ids[:, 5]], tbl_6[ids[:, 6]], tbl_7[ids[:, 7]], tbl_8[ids[:, 8]], tbl_9[ids[:, 9]], tbl_10[ids[:, 10]], tbl_11[ids[:, 11]], tbl_12[ids[:, 12]], tbl_13[ids[:, 13]], tbl_14[ids[:, 14]], tbl_15[ids[:, 15]], tbl_16[ids[:, 16]], tbl_17[ids[:, 17]], tbl_18[ids[:, 18]], tbl_19[ids[:, 19]], tbl_20[ids[:, 20]], tbl_21[ids[:, 21]], tbl_22[ids[:, 22]], tbl_23[ids[:, 23]], tbl_24[ids[:, 24]], tbl_25[ids[:, 25]], tbl_26[ids[:, 26]]], axis=1)
    z = _L0_rec_ref(e, 27)
    z = z.reshape(z.shape[0], -1)
    h = jnp.concatenate([z, dense_ctx], axis=1)
    h = jnp.maximum(h @ W_top1 + b_top1, 0.0)
    h = jnp.maximum(h @ W_top2 + b_top2, 0.0)
    y = h @ W_top3
    return y

_drawn_inputs = setup_inputs


def setup_inputs(seed=0):
    import zlib

    import numpy as np

    out = dict(_drawn_inputs(seed))
    spreads = {'b_top1': (0.0, 0.1), 'b_top2': (0.0, 0.1)}
    factors = {}
    for name, (base, spread) in spreads.items():
        noise = np.random.default_rng([zlib.crc32(name.encode()), seed]).standard_normal(out[name].shape)
        drawn = base * np.exp(spread * noise) if base else spread * noise
        out[name] = jnp.asarray(drawn.astype(out[name].dtype))
    for name, factor in factors.items():
        out[name] = (out[name] * factor).astype(out[name].dtype)
    return out
```

```python
from contextlib import ExitStack

import numpy as np

import concourse.bass as bass
from concourse import mybir

F32 = mybir.dt.float32
U32 = mybir.dt.uint32
ACT = mybir.ActivationFunctionType

P = 128
B = 512
TILES = B // P
NF = 27
D = 128
FP = 32
ND = 16
H1, H2 = 512, 256
C1, C2 = H1 // P, H2 // P
BANK = 512

TG = 4
TGROUPS = [(f, min(TG, NF - f)) for f in range(0, NF, TG)]
NTG = len(TGROUPS)

SG = 4
NGB = 4
GBANKS = P // (SG * NGB)
GPAIR = 2
GSTEPS = GBANKS // GPAIR

MB = 4
BLOCKS = []
_sizes = [(m, min(MB, NF - 1 - m)) for m in range(0, NF - 1, MB)]
_place = {0: (0, 0), 5: (0, 104), 1: (1, 0), 4: (1, 88), 2: (2, 0), 3: (2, 72), 6: (3, 0)}
for _i, (_m, _w) in enumerate(_sizes):
    BLOCKS.append((_m, _w, _m + 1) + _place[_i])
CH = 4
LASTROWS = 4 + ND
CROWS = [P, P, P, LASTROWS]


def w1_rows():
    rows = np.full((CH, P), -1, dtype=np.int64)
    for m0, w, n0, c, p0 in BLOCKS:
        for n in range(n0, NF):
            for j in range(w):
                m = m0 + j
                if m < n:
                    rows[c, p0 + (n - n0) * w + j] = n * (n - 1) // 2 + m
    rows[CH - 1, 4:4 + ND] = NF * (NF - 1) // 2 + np.arange(ND)
    return rows


def build(nc, dense_T, ids, tables, W1, b1, W2, b2, W3, ident_d, out):
    with ExitStack() as ctx:
        def sb(name, shape, dt=F32):
            return ctx.enter_context(nc.sbuf_tensor(name, shape, dt))

        def ps(name, shape, dt=F32):
            return ctx.enter_context(nc.psum_tensor(name, shape, dt))

        def sem(name):
            return ctx.enter_context(nc.semaphore(name))

        ids_sb = sb("ids_sb", [P, TILES, NF], U32)
        ident = sb("ident", [P, P])
        E = sb("E", [P, 2, NF, D])
        eT = sb("eT", [P, 2, P, FP])
        G = sb("G", [FP, 2, NF - 1, P])
        Z = sb("Z", [P, 2, CH - 1, P])
        ZD = sb("ZD", [LASTROWS, B])
        w1 = sb("w1", [P, CH, H1])
        w2 = sb("w2", [P, C1, H2])
        w3 = sb("w3", [P, C2])
        b1s = sb("b1s", [P, C1])
        b2s = sb("b2s", [P, C2])
        h1 = sb("h1", [P, C1, P])
        h2 = sb("h2", [P, C2, P])
        y = sb("y", [1, B])

        psT = [ps(f"psT{i}", [P, TG, P]) for i in range(2)]
        psG = [ps(f"psG{i}", [P, GPAIR, BANK]) for i in range(2)]
        ps1 = ps("ps1", [P, C1, P])
        ps2 = ps("ps2", [P, BANK])

        ids_in = sem("ids_in")
        consts_in = sem("consts_in")
        w_in = sem("w_in")
        pads_set = sem("pads_set")
        rows_in = [[sem(f"rows_in{a}_{k}") for k in range(NTG)] for a in range(2)]
        transposed = sem("transposed")
        eT_act = sem("eT_act")
        eT_dve = sem("eT_dve")
        gram_done = sem("gram_done")
        g_act = sem("g_act")
        g_dve = sem("g_dve")
        z_in = [sem(f"z_in{a}") for a in range(2)]
        l1_done = sem("l1_done")
        h1_ready = sem("h1_ready")
        l2_done = sem("l2_done")
        h2_ready = sem("h2_ready")
        l3_done = sem("l3_done")
        y_ready = sem("y_ready")
        stored = sem("stored")

        block = ctx.enter_context(nc.Block())

        act_k = [k for k in range(NTG) if k % 2 == 0]
        dve_k = [k for k in range(NTG) if k % 2 == 1]

        @block.gpsimd
        def _(pool):
            pool.wait_ge(ids_in, 16)
            for t in range(TILES):
                for k, (f0, n) in enumerate(TGROUPS):
                    if t >= 2:
                        pool.wait_ge(transposed, NTG * (t - 2) + k + 1)
                    for f in range(f0, f0 + n):
                        pool.indirect_dma_start(
                            out=E[:, t % 2, f, :], out_offset=None, in_=tables[f],
                            in_offset=bass.IndirectOffsetOnAxis(ap=ids_sb[:, t, f:f + 1], axis=0),
                        ).then_inc(rows_in[t % 2][k], 16)

        @block.sync
        def _(sp):
            sp.dma_start(ids_sb[:, :, :], ids.rearrange("(t p) f -> p t f", p=P)).then_inc(ids_in, 16)
            sp.dma_start(ident[:, :], ident_d).then_inc(consts_in, 16)
            sp.dma_start(w1[:, 0:CH - 1, :], W1[0:(CH - 1) * P, :].rearrange("(c p) n -> p c n", p=P)).then_inc(w_in, 16)
            sp.dma_start(w1[0:LASTROWS, CH - 1, :], W1[(CH - 1) * P:(CH - 1) * P + LASTROWS, :]).then_inc(w_in, 16)
            sp.dma_start(w2[:, :, :], W2.rearrange("(c p) n -> p c n", p=P)).then_inc(w_in, 16)
            sp.dma_start(w3[:, :], W3).then_inc(w_in, 16)
            sp.dma_start(b1s[:, :], b1).then_inc(w_in, 16)
            sp.dma_start(b2s[:, :], b2).then_inc(w_in, 16)
            sp.dma_start(ZD[4:LASTROWS, :], dense_T).then_inc(w_in, 16)
            for t in range(TILES):
                a = t % 2
                sp.wait_ge(g_act, 2 * GSTEPS * (t + 1))
                sp.wait_ge(g_dve, 2 * GSTEPS * (t + 1))
                if t >= 2:
                    sp.wait_ge(l1_done, t - 1)
                for m0, w, n0, c, p0 in BLOCKS:
                    rows = (NF - n0) * w
                    dst = Z[p0:p0 + rows, a, c, :] if c < CH - 1 else ZD[0:rows, t * P:(t + 1) * P]
                    sp.dma_start(dst, G[n0:NF, a, m0:m0 + w, :]).then_inc(z_in[a], 16)
            sp.wait_ge(y_ready, TILES)
            sp.dma_start(out, y[0:1, :]).then_inc(stored, 16)
            sp.wait_ge(stored, 16)

        @block.tensor
        def _(pe):
            pe.wait_ge(consts_in, 16)
            for t in range(TILES):
                a = t % 2
                for k, (f0, n) in enumerate(TGROUPS):
                    pe.wait_ge(rows_in[a][k], 16 * n * (t // 2 + 1))
                    i = NTG * t + k
                    if i >= 2:
                        j = i - 2
                        if (j % NTG) % 2 == 0:
                            pe.wait_ge(eT_act, len(act_k) * (j // NTG) + (j % NTG) // 2 + 1)
                        else:
                            pe.wait_ge(eT_dve, len(dve_k) * (j // NTG) + (j % NTG) // 2 + 1)
                    for q in range(n):
                        last = nc.tensor.transpose(psT[i % 2][:, q, :], E[:, a, f0 + q, :], ident[:, :])
                    last.then_inc(transposed, 1)
                pe.wait_ge(eT_act, len(act_k) * (t + 1))
                pe.wait_ge(eT_dve, len(dve_k) * (t + 1))
                if t == 0:
                    pe.wait_ge(pads_set, 1)
                for s in range(GSTEPS):
                    i = GSTEPS * t + s
                    if i >= 2:
                        pe.wait_ge(g_act, 2 * (i - 1))
                        pe.wait_ge(g_dve, 2 * (i - 1))
                    for bk in range(GPAIR):
                        for r in range(NGB):
                            b0 = SG * (NGB * (GPAIR * s + bk) + r)
                            last = nc.tensor.matmul(
                                psG[i % 2][:, bk, r * SG * (NF - 1):(r + 1) * SG * (NF - 1)],
                                eT[:, a, b0:b0 + SG, :].rearrange("p s f -> p (s f)"),
                                eT[:, a, b0:b0 + SG, 0:NF - 1], start=True, stop=True)
                    last.then_inc(gram_done, 1)
                if t == 0:
                    pe.wait_ge(w_in, 7 * 16)
                pe.wait_ge(z_in[a], 16 * len(BLOCKS) * (t // 2 + 1))
                for h in range(C1):
                    for c in range(CH):
                        K = CROWS[c]
                        rhs = Z[0:K, a, c, :] if c < CH - 1 else ZD[:, t * P:(t + 1) * P]
                        last = nc.tensor.matmul(ps1[:, h, :], w1[0:K, c, h * P:(h + 1) * P], rhs,
                                                start=(c == 0), stop=(c == CH - 1))
                last.then_inc(l1_done, 1)
                pe.wait_ge(h1_ready, C1 * (t + 1))
                for h in range(C2):
                    for c in range(C1):
                        last = nc.tensor.matmul(ps2[:, h * P:(h + 1) * P], w2[:, c, h * P:(h + 1) * P], h1[:, c, :],
                                                start=(c == 0), stop=(c == C1 - 1))
                last.then_inc(l2_done, 1)
                pe.wait_ge(h2_ready, C2 * (t + 1))
                for c in range(C2):
                    last = nc.tensor.matmul(ps2[0:1, C2 * P:(C2 + 1) * P], w3[:, c:c + 1], h2[:, c, :],
                                            start=(c == 0), stop=(c == C2 - 1))
                last.then_inc(l3_done, 1)

        def evacuate_eT(eng, copy, t, k, done):
            f0, n = TGROUPS[k]
            i = NTG * t + k
            eng.wait_ge(transposed, i + 1)
            copy(eT[:, t % 2, :, f0:f0 + n].rearrange("p b f -> p f b"), psT[i % 2][:, 0:n, :]).then_inc(done, 1)

        def evacuate_gram(eng, copy, t, s, q, done):
            i = GSTEPS * t + s
            W = SG * (NF - 1)
            src = psG[i % 2][FP * q:FP * q + NF, :, 0:NGB * W].rearrange(
                "p k (r s m) -> p k r s m", r=NGB, s=SG)[:, :, :, q, :]
            b0 = SG * NGB * GPAIR * s
            dst = G[0:NF, t % 2, :, b0:b0 + SG * NGB * GPAIR].rearrange(
                "p m (k r s) -> p k r s m", k=GPAIR, r=NGB)[:, :, :, q, :]
            copy(dst, src).then_inc(done, 1)

        @block.scalar
        def _(act):
            for t in range(TILES):
                for k in act_k:
                    evacuate_eT(act, nc.scalar.copy, t, k, eT_act)
                if t >= 2:
                    act.wait_ge(z_in[t % 2], 16 * len(BLOCKS) * (t // 2))
                for s in range(GSTEPS):
                    act.wait_ge(gram_done, GSTEPS * t + s + 1)
                    for q in (2, 3):
                        evacuate_gram(act, nc.scalar.copy, t, s, q, g_act)
                act.wait_ge(l1_done, t + 1)
                if t == 0:
                    act.wait_ge(w_in, 7 * 16)
                for c in range(C1):
                    nc.scalar.activation(h1[:, c, :], ps1[:, c, :], ACT.Relu, bias=b1s[:, c:c + 1]).then_inc(h1_ready, 1)
                act.wait_ge(l2_done, t + 1)
                for c in range(C2):
                    nc.scalar.activation(h2[:, c, :], ps2[:, c * P:(c + 1) * P], ACT.Relu,
                                         bias=b2s[:, c:c + 1]).then_inc(h2_ready, 1)
                act.wait_ge(l3_done, t + 1)
                nc.scalar.copy(y[0:1, t * P:(t + 1) * P], ps2[0:1, C2 * P:(C2 + 1) * P]).then_inc(y_ready, 1)

        @block.vector
        def _(dve):
            for a in range(2):
                last = nc.vector.memset(eT[:, a, :, NF:FP], 0.0)
            last.then_inc(pads_set, 1)
            for t in range(TILES):
                for k in dve_k:
                    evacuate_eT(dve, nc.vector.tensor_copy, t, k, eT_dve)
                if t >= 2:
                    dve.wait_ge(z_in[t % 2], 16 * len(BLOCKS) * (t // 2))
                for s in range(GSTEPS):
                    dve.wait_ge(gram_done, GSTEPS * t + s + 1)
                    for q in (0, 1):
                        evacuate_gram(dve, nc.vector.tensor_copy, t, s, q, g_dve)


def kernel(**inputs):
    import concourse.bacc as bacc
    from concourse.bass_utils import run_bass_kernel_spmd

    nc = bacc.Bacc("TRN2", target_bir_lowering=False, num_devices=1)
    arrays = {}

    def dram(name, a):
        a = np.ascontiguousarray(a)
        arrays["in_" + name] = a
        return nc.dram_tensor("in_" + name, a.shape, mybir.dt.from_np(a.dtype), kind="ExternalInput").ap()

    dense_T = dram("dense_T", np.asarray(inputs["dense_ctx"]).T)
    ids = dram("ids", np.asarray(inputs["ids"]).view(np.uint32))
    tables = [dram(f"tbl_{f}", inputs[f"tbl_{f}"]) for f in range(NF)]
    rows = w1_rows().reshape(-1)
    w1 = np.zeros((CH * P, H1), np.float32)
    w1[rows >= 0] = np.asarray(inputs["W_top1"])[rows[rows >= 0]]
    W1 = dram("W1", w1)
    b1 = dram("b1", np.asarray(inputs["b_top1"]).reshape(C1, P).T)
    W2 = dram("W2", inputs["W_top2"])
    b2 = dram("b2", np.asarray(inputs["b_top2"]).reshape(C2, P).T)
    W3 = dram("W3", np.asarray(inputs["W_top3"]).reshape(C2, P).T)
    ident = dram("ident", np.eye(P, dtype=np.float32))
    out = nc.dram_tensor("out", (B, 1), F32, kind="ExternalOutput").ap()
    build(nc, dense_T, ids, tables, W1, b1, W2, b2, W3, ident, out.rearrange("b o -> o b"))
    r = run_bass_kernel_spmd(nc, [arrays], core_ids=[0])
    return r.results[0]["out"]
```

```python
from contextlib import ExitStack

import numpy as np

import concourse.bass as bass
from concourse import mybir

F32 = mybir.dt.float32
F32R = mybir.dt.float32r
U32 = mybir.dt.uint32
I32 = mybir.dt.int32
ACT = mybir.ActivationFunctionType
ALU = mybir.AluOpType

P = 128
B = 512
TILES = B // P
NF = 27
D = 128
FP = 32
ND = 16
H1, H2 = 512, 256
C1, C2 = H1 // P, H2 // P
BANK = 512

OR = 1000
OP = 125
OQ = OR // OP
NOH = 10
ONEHOT = [26, 25, 24, 23, 22, 20, 19, 17, 13, 8][:NOH]
GATHER = [f for f in range(NF) if f not in ONEHOT]
NGA = len(GATHER)
FIELD_AT = ONEHOT + GATHER

TG = 4
TGROUPS = [(g, min(TG, NGA - g)) for g in range(0, NGA, TG)]
NTG = len(TGROUPS)

SG = 4
NM = NF - 1
NGB = 4
GPAIR = 2
GSTEPS = P // (SG * NGB * GPAIR)
SSTEP = SG * NGB * GPAIR

MB = 4
BLOCKS = []
_place = {0: (0, 0), 5: (0, 104), 1: (1, 0), 4: (1, 88), 2: (2, 0), 3: (2, 72), 6: (3, 0)}
for _i, _m in enumerate(range(0, NM, MB)):
    BLOCKS.append((_m, min(MB, NM - _m), _m + 1) + _place[_i])
CH = 4
LASTPAIRS = 4
LASTROWS = LASTPAIRS + ND
CROWS = [P, P, P, LASTROWS]


def w1_rows():
    rows = np.full((CH, P), -1, dtype=np.int64)
    for m0, w, n0, c, p0 in BLOCKS:
        for n in range(n0, NF):
            for j in range(w):
                m = m0 + j
                if m < n:
                    hi, lo = max(FIELD_AT[n], FIELD_AT[m]), min(FIELD_AT[n], FIELD_AT[m])
                    rows[c, p0 + (n - n0) * w + j] = hi * (hi - 1) // 2 + lo
    rows[CH - 1, LASTPAIRS:LASTROWS] = NF * (NF - 1) // 2 + np.arange(ND)
    return rows


def program_order():
    turns = [("turn", t, k) for t in range(TILES) for k in range(NTG)]
    order = []
    for j in range(NOH):
        order.append(("onehot", j, 0))
        if turns and turns[0][1] < 2:
            order.append(turns.pop(0))
    order += [x for x in turns if x[1] < 2]
    turns = [x for x in turns if x[1] >= 2]
    grams = lambda t: [("gram", t, s) for s in range(GSTEPS)]
    order += grams(0) + turns[:3] + grams(1) + turns[3:NTG] + [("layers", 0, 0)] + turns[NTG:NTG + 1]
    order += [("layers", 1, 0)] + grams(2) + turns[NTG + 1:] + grams(3)
    order += [("layers", 2, 0), ("layers", 3, 0)]
    return order


ORDER = program_order()


def act_turns(i):
    return i < 2 * NTG or i % 2 == 0


def turned(i):
    n = sum(act_turns(x) for x in range(i + 1))
    return n, i + 1 - n


def build(nc, dense_T, ids, ids_T, rowno, tables, W1, b1, W2, b2, W3, ident_d, out):
    with ExitStack() as ctx:
        def sb(name, shape, dt=F32):
            return ctx.enter_context(nc.sbuf_tensor(name, shape, dt))

        def ps(name, shape, dt=F32):
            return ctx.enter_context(nc.psum_tensor(name, shape, dt))

        def sem(name):
            return ctx.enter_context(nc.semaphore(name))

        ids_sb = sb("ids_sb", [P, TILES, NF], U32)
        ident = sb("ident", [P, P])
        rown = sb("rown", [OP, OQ])
        idb = sb("idb", [OP, 2, B], I32)
        raw = sb("raw", [OP, 2, OQ * D])
        hi = sb("hi", [OP, 2, OQ * D], F32R)
        lo = sb("lo", [OP, 2, OQ * D], F32R)
        pick = sb("pick", [OP, 2, OQ, B], F32R)
        E = sb("E", [P, 2, NGA, D])
        eT = sb("eT", [P, TILES, P, FP])
        G = sb("G", [NF, 2, NM, P])
        Z = sb("Z", [P, 2, CH - 1, P])
        ZD = sb("ZD", [LASTROWS, B])
        w1 = sb("w1", [P, CH, H1])
        w2 = sb("w2", [P, C1, H2])
        w3 = sb("w3", [P, C2])
        b1s = sb("b1s", [P, C1])
        b2s = sb("b2s", [P, C2])
        h1 = sb("h1", [P, C1, P])
        h2 = sb("h2", [P, C2, P])
        y = sb("y", [1, B])

        psT = [ps(f"psT{i}", [P, TG, P]) for i in range(2)]
        psG = [ps(f"psG{i}", [P, GPAIR, BANK]) for i in range(2)]
        psA = ps("psA", [P, BANK])
        psB = ps("psB", [P, BANK])
        psO = [psG[0][:, 0, :], psG[0][:, 1, :], psG[1][:, 0, :], psG[1][:, 1, :]]
        y_ps = psA[0:1, 3 * P:4 * P]

        ids_in = sem("ids_in")
        rown_in = sem("rown_in")
        ident_in = sem("ident_in")
        w_in = sem("w_in")
        pads_set = sem("pads_set")
        raw_in = [sem(f"raw_in{a}") for a in range(2)]
        idb_in = [sem(f"idb_in{a}") for a in range(2)]
        hi_ready = sem("hi_ready")
        lo_ready = sem("lo_ready")
        pick_ready = sem("pick_ready")
        picked = sem("picked")
        picked_out = sem("picked_out")
        rows_in = [[sem(f"rows_in{a}_{k}") for k in range(NTG)] for a in range(2)]
        transposed = sem("transposed")
        eT_act = sem("eT_act")
        eT_dve = sem("eT_dve")
        gram_done = sem("gram_done")
        g_act = sem("g_act")
        g_dve = sem("g_dve")
        z_in = [sem(f"z_in{a}") for a in range(2)]
        l1a_done = sem("l1a_done")
        l1b_done = sem("l1b_done")
        h1_act = sem("h1_act")
        h1_dve = sem("h1_dve")
        l2a_done = sem("l2a_done")
        l2b_done = sem("l2b_done")
        h2_act = sem("h2_act")
        h2_dve = sem("h2_dve")
        l3_done = sem("l3_done")
        y_ready = sem("y_ready")
        stored = sem("stored")
        NW = 7

        block = ctx.enter_context(nc.Block())

        @block.gpsimd
        def _(pool):
            pool.wait_ge(ids_in, 16)
            for t in range(TILES):
                for k, (g0, n) in enumerate(TGROUPS):
                    if t >= 2:
                        pool.wait_ge(transposed, NTG * (t - 2) + k + 1)
                    for g in range(g0, g0 + n):
                        f = GATHER[g]
                        pool.indirect_dma_start(
                            out=E[:, t % 2, g, :], out_offset=None, in_=tables[f],
                            in_offset=bass.IndirectOffsetOnAxis(ap=ids_sb[:, t, f:f + 1], axis=0),
                        ).then_inc(rows_in[t % 2][k], 16)

        @block.sync
        def _(sp):
            sp.dma_start(ids_sb[:, :, :], ids.rearrange("(t p) f -> p t f", p=P)).then_inc(ids_in, 16)
            for j, f in enumerate(ONEHOT):
                a = j % 2
                if j >= 2:
                    sp.wait_ge(lo_ready, j - 1)
                    sp.wait_ge(pick_ready, OQ * (j - 1))
                sp.dma_start(raw[:, a, :], tables[f].rearrange("(p q) d -> p (q d)", q=OQ)).then_inc(raw_in[a], 16)
                sp.dma_start(idb[:, a, :], ids_T[f:f + 1, :].to_broadcast([OP, B])).then_inc(idb_in[a], 16)
                if j == 0:
                    sp.dma_start(rown[:, :], rowno).then_inc(rown_in, 16)
                if j == 1:
                    sp.dma_start(ident[:, :], ident_d).then_inc(ident_in, 16)
            sp.dma_start(w1[:, 0:CH - 1, :], W1[0:(CH - 1) * P, :].rearrange("(c p) n -> p c n", p=P)).then_inc(w_in, 16)
            sp.dma_start(w1[0:LASTROWS, CH - 1, :], W1[(CH - 1) * P:(CH - 1) * P + LASTROWS, :]).then_inc(w_in, 16)
            sp.dma_start(w2[:, :, :], W2.rearrange("(c p) n -> p c n", p=P)).then_inc(w_in, 16)
            sp.dma_start(w3[:, :], W3).then_inc(w_in, 16)
            sp.dma_start(b1s[:, :], b1).then_inc(w_in, 16)
            sp.dma_start(b2s[:, :], b2).then_inc(w_in, 16)
            sp.dma_start(ZD[LASTPAIRS:LASTROWS, :], dense_T).then_inc(w_in, 16)
            for t in range(TILES):
                a = t % 2
                sp.wait_ge(g_act, 2 * GSTEPS * (t + 1))
                sp.wait_ge(g_dve, 2 * GSTEPS * (t + 1))
                if t >= 2:
                    sp.wait_ge(l1b_done, t - 1)
                for m0, w, n0, c, p0 in BLOCKS:
                    rows = (NF - n0) * w
                    dst = Z[p0:p0 + rows, a, c, :] if c < CH - 1 else ZD[0:rows, t * P:(t + 1) * P]
                    sp.dma_start(dst, G[n0:NF, a, m0:m0 + w, :]).then_inc(z_in[a], 16)
            sp.wait_ge(y_ready, TILES)
            sp.dma_start(out, y[0:1, :]).then_inc(stored, 16)
            sp.wait_ge(stored, 16)

        @block.tensor
        def _(pe):
            def pick_field(j):
                if j == 0:
                    pe.wait_ge(lo_ready, 1)
                if j >= 4:
                    pe.wait_ge(picked_out, j - 3)
                pe.wait_ge(hi_ready, j + 1)
                for q in range(OQ):
                    pe.wait_ge(pick_ready, OQ * j + q + 1)
                    for half in (hi, lo):
                        last = nc.tensor.matmul(psO[j % 4], half[:, j % 2, q * D:(q + 1) * D],
                                                pick[:, j % 2, q, :], start=(q == 0 and half is hi),
                                                stop=(q == OQ - 1 and half is lo))
                last.then_inc(picked, 1)

            def turn(t, k):
                g0, n = TGROUPS[k]
                i = NTG * t + k
                if i == 0:
                    pe.wait_ge(ident_in, 16)
                pe.wait_ge(rows_in[t % 2][k], 16 * n * (t // 2 + 1))
                if i >= 2:
                    by_act, by_dve = turned(i - 2)
                    if act_turns(i - 2):
                        pe.wait_ge(eT_act, by_act)
                    else:
                        pe.wait_ge(eT_dve, by_dve)
                for g in range(n):
                    last = nc.tensor.transpose(psT[i % 2][:, g, :], E[:, t % 2, g0 + g, :], ident[:, :])
                last.then_inc(transposed, 1)

            def gram(t, s):
                i = GSTEPS * t + s
                if i == 0:
                    pe.wait_ge(pads_set, 1)
                    pe.wait_ge(picked_out, NOH)
                if s == 0:
                    by_act, by_dve = turned(NTG * (t + 1) - 1)
                    pe.wait_ge(eT_act, by_act)
                    if by_dve:
                        pe.wait_ge(eT_dve, by_dve)
                if i >= 2:
                    pe.wait_ge(g_act, 2 * (i - 1))
                    pe.wait_ge(g_dve, 2 * (i - 1))
                for bk in range(GPAIR):
                    for r in range(NGB):
                        b0 = SSTEP * s + SG * (NGB * bk + r)
                        last = nc.tensor.matmul(
                            psG[i % 2][:, bk, r * SG * NM:(r + 1) * SG * NM],
                            eT[:, t, b0:b0 + SG, :].rearrange("p s f -> p (s f)"),
                            eT[:, t, b0:b0 + SG, 0:NM], start=True, stop=True)
                last.then_inc(gram_done, 1)

            def layers(t):
                if t == 0:
                    pe.wait_ge(w_in, NW * 16)
                else:
                    pe.wait_ge(y_ready, t)
                pe.wait_ge(z_in[t % 2], 16 * len(BLOCKS) * (t // 2 + 1))
                for h in range(C1):
                    bank, done = (psA, l1a_done) if h < C1 // 2 else (psB, l1b_done)
                    col = (h % (C1 // 2)) * P
                    for c in range(CH):
                        K = CROWS[c]
                        rhs = Z[0:K, t % 2, c, :] if c < CH - 1 else ZD[:, t * P:(t + 1) * P]
                        last = nc.tensor.matmul(bank[:, col:col + P], w1[0:K, c, h * P:(h + 1) * P], rhs,
                                                start=(c == 0), stop=(c == CH - 1))
                    if h % (C1 // 2) == C1 // 2 - 1:
                        last.then_inc(done, 1)
                for h, bank, done in ((0, psA, l2a_done), (1, psB, l2b_done)):
                    for c in range(C1):
                        if h == 0 and c == 0:
                            pe.wait_ge(h1_act, C1 // 2 * (t + 1))
                        if h == 0 and c == C1 // 2:
                            pe.wait_ge(h1_dve, C1 // 2 * (t + 1))
                        last = nc.tensor.matmul(bank[:, 2 * P:3 * P], w2[:, c, h * P:(h + 1) * P], h1[:, c, :],
                                                start=(c == 0), stop=(c == C1 - 1))
                    last.then_inc(done, 1)
                for c, ready in ((0, h2_act), (1, h2_dve)):
                    pe.wait_ge(ready, t + 1)
                    last = nc.tensor.matmul(y_ps, w3[:, c:c + 1], h2[:, c, :], start=(c == 0), stop=(c == C2 - 1))
                last.then_inc(l3_done, 1)

            for kind, x, i in ORDER:
                if kind == "onehot":
                    pick_field(x)
                elif kind == "turn":
                    turn(x, i)
                elif kind == "gram":
                    gram(x, i)
                else:
                    layers(x)

        def turn_out(eng, copy, t, k, done):
            g0, n = TGROUPS[k]
            i = NTG * t + k
            eng.wait_ge(transposed, i + 1)
            copy(eT[:, t, :, NOH + g0:NOH + g0 + n].rearrange("p b f -> p f b"), psT[i % 2][:, 0:n, :]).then_inc(done, 1)

        def gram_out(eng, copy, t, s, samples, done):
            i = GSTEPS * t + s
            if s == 0 and t >= 2:
                eng.wait_ge(z_in[t % 2], 16 * len(BLOCKS) * (t // 2))
            eng.wait_ge(gram_done, i + 1)
            for q in samples:
                src = psG[i % 2][FP * q:FP * q + NF, :, 0:NGB * SG * NM].rearrange(
                    "p k (r s m) -> p k r s m", r=NGB, s=SG)[:, :, :, q, :]
                dst = G[:, t % 2, :, SSTEP * s:SSTEP * (s + 1)].rearrange(
                    "p m (k r s) -> p k r s m", k=GPAIR, r=NGB)[:, :, :, q, :]
                copy(dst, src).then_inc(done, 1)

        @block.scalar
        def _(act):
            def split_hi(j):
                act.wait_ge(raw_in[j % 2], 16 * (j // 2 + 1))
                if j >= 2:
                    act.wait_ge(picked, j - 1)
                nc.scalar.copy(hi[:, j % 2, :], raw[:, j % 2, :]).then_inc(hi_ready, 1)

            split_hi(0)
            split_hi(1)
            for kind, x, i in ORDER:
                if kind == "onehot":
                    act.wait_ge(picked, x + 1)
                    nc.scalar.copy(eT[:, :, :, x], psO[x % 4].rearrange("p (t b) -> p t b", b=P)).then_inc(picked_out, 1)
                    if x + 2 < NOH:
                        split_hi(x + 2)
                elif kind == "turn":
                    if act_turns(NTG * x + i):
                        turn_out(act, nc.scalar.copy, x, i, eT_act)
                elif kind == "gram":
                    gram_out(act, nc.scalar.copy, x, i, (2, 3), g_act)
                else:
                    t = x
                    act.wait_ge(l1a_done, t + 1)
                    if t == 0:
                        act.wait_ge(w_in, NW * 16)
                    for c in range(C1 // 2):
                        nc.scalar.activation(h1[:, c, :], psA[:, c * P:(c + 1) * P], ACT.Relu,
                                             bias=b1s[:, c:c + 1]).then_inc(h1_act, 1)
                    act.wait_ge(l2a_done, t + 1)
                    nc.scalar.activation(h2[:, 0, :], psA[:, 2 * P:3 * P], ACT.Relu,
                                         bias=b2s[:, 0:1]).then_inc(h2_act, 1)
                    act.wait_ge(l3_done, t + 1)
                    nc.scalar.copy(y[0:1, t * P:(t + 1) * P], y_ps).then_inc(y_ready, 1)

        @block.vector
        def _(dve):
            def make_pick(j):
                dve.wait_ge(hi_ready, j + 1)
                dve.wait_ge(raw_in[j % 2], 16 * (j // 2 + 1))
                if j >= 2:
                    dve.wait_ge(picked, j - 1)
                nc.vector.tensor_tensor(lo[:, j % 2, :], raw[:, j % 2, :], hi[:, j % 2, :].bitcast(F32),
                                        ALU.subtract).then_inc(lo_ready, 1)
                if j == 0:
                    dve.wait_ge(rown_in, 16)
                dve.wait_ge(idb_in[j % 2], 16 * (j // 2 + 1))
                for q in range(OQ):
                    nc.vector.tensor_scalar(pick[:, j % 2, q, :], idb[:, j % 2, :], rown[:, q:q + 1], None,
                                            ALU.is_equal).then_inc(pick_ready, 1)

            nc.vector.memset(eT[:, :, :, NF:FP], 0.0).then_inc(pads_set, 1)
            make_pick(0)
            make_pick(1)
            for kind, x, i in ORDER:
                if kind == "onehot":
                    if x + 2 < NOH:
                        make_pick(x + 2)
                elif kind == "turn":
                    if not act_turns(NTG * x + i):
                        turn_out(dve, nc.vector.tensor_copy, x, i, eT_dve)
                elif kind == "gram":
                    gram_out(dve, nc.vector.tensor_copy, x, i, (0, 1), g_dve)
                else:
                    t = x
                    dve.wait_ge(l1b_done, t + 1)
                    if t == 0:
                        dve.wait_ge(w_in, NW * 16)
                    for c in range(C1 // 2, C1):
                        col = (c - C1 // 2) * P
                        nc.vector.tensor_scalar(h1[:, c, :], psB[:, col:col + P], b1s[:, c:c + 1], 0.0,
                                                ALU.add, ALU.max).then_inc(h1_dve, 1)
                    dve.wait_ge(l2b_done, t + 1)
                    nc.vector.tensor_scalar(h2[:, 1, :], psB[:, 2 * P:3 * P], b2s[:, 1:2], 0.0,
                                            ALU.add, ALU.max).then_inc(h2_dve, 1)


def kernel(**inputs):
    import concourse.bacc as bacc
    from concourse.bass_utils import run_bass_kernel_spmd

    nc = bacc.Bacc("TRN2", target_bir_lowering=False, num_devices=1)
    arrays = {}

    def dram(name, a):
        a = np.ascontiguousarray(a)
        arrays["in_" + name] = a
        return nc.dram_tensor("in_" + name, a.shape, mybir.dt.from_np(a.dtype), kind="ExternalInput").ap()

    dense_T = dram("dense_T", np.asarray(inputs["dense_ctx"]).T)
    ids = dram("ids", np.asarray(inputs["ids"]).view(np.uint32))
    ids_T = dram("ids_T", np.asarray(inputs["ids"]).T)
    rowno = dram("rowno", np.arange(OR, dtype=np.float32).reshape(OP, OQ))
    tables = [dram(f"tbl_{f}", inputs[f"tbl_{f}"]) for f in range(NF)]
    rows = w1_rows().reshape(-1)
    w1 = np.zeros((CH * P, H1), np.float32)
    w1[rows >= 0] = np.asarray(inputs["W_top1"])[rows[rows >= 0]]
    W1 = dram("W1", w1)
    b1 = dram("b1", np.asarray(inputs["b_top1"]).reshape(C1, P).T)
    W2 = dram("W2", inputs["W_top2"])
    b2 = dram("b2", np.asarray(inputs["b_top2"]).reshape(C2, P).T)
    W3 = dram("W3", np.asarray(inputs["W_top3"]).reshape(C2, P).T)
    ident = dram("ident", np.eye(P, dtype=np.float32))
    out = nc.dram_tensor("out", (B, 1), F32, kind="ExternalOutput").ap()
    build(nc, dense_T, ids, ids_T, rowno, tables, W1, b1, W2, b2, W3, ident, out.rearrange("b o -> o b"))
    r = run_bass_kernel_spmd(nc, [arrays], core_ids=[0])
    return r.results[0]["out"]
```

```python
from contextlib import ExitStack

import numpy as np

import concourse.bass as bass
from concourse import mybir

F32 = mybir.dt.float32
F32R = mybir.dt.float32r
BF16 = mybir.dt.bfloat16
U32 = mybir.dt.uint32
I32 = mybir.dt.int32
ACT = mybir.ActivationFunctionType
ALU = mybir.AluOpType

P = 128
B = 512
TILES = B // P
NF = 27
D = 128
FP = 32
ND = 16
H1, H2 = 512, 256
C1, C2 = H1 // P, H2 // P
BANK = 512

OR = 1000
OP = 125
OQ = OR // OP
HALF = OQ * D // 2
ONEHOT = [26, 25, 24, 23, 22, 20, 19, 17, 13, 8]
NOH = len(ONEHOT)
WARMUP = 10
GATHER = [f for f in range(NF) if f not in ONEHOT]
NGA = len(GATHER)
FIELD_AT = ONEHOT + GATHER

TG = 4
TGROUPS = [(g, min(TG, NGA - g)) for g in range(0, NGA, TG)]
NTG = len(TGROUPS)
FLIPS = [(2, 0), (2, 1), (2, 2), (2, 3), (3, 0), (3, 1), (3, 2)]
BLOCK = 32
NBLOCK = P // BLOCK

SG = 4
GC = (SG - 1) * FP + NF
NM = NF - 1
NGB = 4
GPAIR = 2
GSTEPS = P // (SG * NGB * GPAIR)
SSTEP = SG * NGB * GPAIR

CHUNKS = [(0, 4, 1), (4, 5, 5), (9, 6, 9), (15, 11, 16)]
CH = len(CHUNKS)
PAIRS = [(NF - n0) * w for _, w, n0 in CHUNKS]
CROWS = [PAIRS[0] + ND] + PAIRS[1:]
assert max(CROWS) <= P and sum(w for _, w, _ in CHUNKS) == NM


def w1_rows():
    rows = np.full((CH, P), -1, dtype=np.int64)
    for c, (m0, w, n0) in enumerate(CHUNKS):
        for n in range(n0, NF):
            for m in range(m0, min(m0 + w, n)):
                hi, lo = max(FIELD_AT[n], FIELD_AT[m]), min(FIELD_AT[n], FIELD_AT[m])
                rows[c, (n - n0) * w + m - m0] = hi * (hi - 1) // 2 + lo
    rows[0, PAIRS[0]:CROWS[0]] = NF * (NF - 1) // 2 + np.arange(ND)
    return rows


def program_order():
    turns = [[("turn", t, k) for k in range(NTG) if (t, k) not in FLIPS] for t in range(TILES)]
    flips = [[("flip", t, (k, half)) for k in range(NTG) if (t, k) in FLIPS for half in range(2)]
             for t in range(TILES)]
    gram = [[("gram", t, s) for s in range(GSTEPS)] for t in range(TILES)]
    l1, l2, l3 = ([(x, t, 0) for t in range(TILES)] for x in ("layer1", "layer2", "layer3"))
    beside = {j: [turn] for j, turn in enumerate(turns[0])}
    beside.update({NOH - 4: turns[1][:1], NOH - 3: turns[1][1:2], NOH - 2: turns[1][2:3],
                   NOH - 1: turns[1][3:]})
    order = []
    for j in range(NOH):
        order += [("onehot", j, 0)] + beside.get(j, [])
    order += flips[2] + gram[0] + gram[1] + turns[2] + [l1[0]]
    order += gram[2][:1] + flips[3][:2] + [l2[0]] + gram[2][1:2] + [l3[0]] + gram[2][2:3] + flips[3][2:4] + [l1[1]]
    order += flips[3][4:6] + gram[2][3:] + turns[3][:1] + [l2[1]] + turns[3][1:] + [l3[1]]
    order += gram[3] + [l1[2], l1[3], l2[2], l2[3], l3[2], l3[3]]
    return order


ORDER = program_order()
TURNS = [(t, k) for kind, t, k in ORDER if kind == "turn"]


def gram_quadrants(t):
    return ((0, 1, 2, 3), ()) if t < TILES - 1 else ((2, 3), (0, 1))


def copies(engine, t, s):
    return sum(len(gram_quadrants(u)[engine]) * GSTEPS for u in range(t)) + len(gram_quadrants(t)[engine]) * (s + 1)


def build(nc, dense_T, ids, ids_T, tables, W1, b1, W2, b2, W3, ident_d, out):
    with ExitStack() as ctx:
        def sb(name, shape, dt=F32):
            return ctx.enter_context(nc.sbuf_tensor(name, shape, dt))

        def ps(name, shape, dt=F32):
            return ctx.enter_context(nc.psum_tensor(name, shape, dt))

        def sem(name):
            return ctx.enter_context(nc.semaphore(name))

        ids_sb = sb("ids_sb", [P, TILES, NF], U32)
        ident = sb("ident", [P, P])
        rown = sb("rown", [OP, OQ])
        idb = sb("idb", [OP, 2, B], I32)
        raw = sb("raw", [OP, 2, OQ * D])
        hi = sb("hi", [OP, 2, OQ * D], F32R)
        lo = sb("lo", [OP, 2, OQ * D], F32R)
        pick = sb("pick", [OP, 2, OQ, B], F32R)
        E = sb("E", [P, 2, NGA, D])
        eT = sb("eT", [P, TILES, P, FP])
        G = sb("G", [NF, 2, NM, P])
        Z = sb("Z", [P, CH, B])
        w1 = sb("w1", [P, CH, H1])
        w2 = sb("w2", [P, C1, H2])
        w3 = sb("w3", [P, C2])
        b1s = sb("b1s", [P, C1])
        b2s = sb("b2s", [P, C2])
        h1 = sb("h1", [P, 2, C1, P])
        h2 = sb("h2", [P, 2, C2, P])
        y = sb("y", [1, B])

        zeros = sb("zeros", [P, BANK], BF16)
        psT = [ps(f"psT{i}", [P, TG, P]) for i in range(2)]
        dist = sb("dist", [OP, B])
        psG = [ps(f"psG{i}", [P, GPAIR, BANK]) for i in range(2)]
        psA = ps("psA", [P, BANK])
        psB = ps("psB", [P, BANK])
        psO = [psG[0][:, 0, :], psG[0][:, 1, :], psG[1][:, 0, :], psG[1][:, 1, :]]

        def layer_psum(t):
            if t < TILES - 1:
                return [psA[:, 0:P], psA[:, P:2 * P], psB[:, 0:P], psB[:, P:2 * P]], \
                    [psA[:, 2 * P:3 * P], psB[:, 2 * P:3 * P]], psA[0:1, 3 * P:4 * P]
            return [o[:, 0:P] for o in psO], [psO[0][:, P:2 * P], psO[2][:, P:2 * P]], psO[0][0:1, 2 * P:3 * P]

        ids_in = sem("ids_in")
        rown_set = sem("rown_set")
        ident_in = sem("ident_in")
        w_in = sem("w_in")
        zeros_set = sem("zeros_set")
        pads_set = sem("pads_set")
        raw0_in = sem("raw0_in")
        raw_in = [sem(f"raw_in{a}") for a in range(2)]
        idb_in = [sem(f"idb_in{a}") for a in range(2)]
        hi0_ready = sem("hi0_ready")
        hi_ready = sem("hi_ready")
        lo_ready = sem("lo_ready")
        pick_ready = sem("pick_ready")
        dist_ready = sem("dist_ready")
        pick_act = sem("pick_act")
        picked = sem("picked")
        picked_out = sem("picked_out")
        rows_in = [[sem(f"rows_in{a}_{k}") for k in range(NTG)] for a in range(2)]
        transposed = sem("transposed")
        eT_act = sem("eT_act")
        flipped = sem("flipped")
        gram_done = sem("gram_done")
        g_act = sem("g_act")
        g_dve = sem("g_dve")
        z_in = [sem(f"z_in{t}") for t in range(TILES - 1)]
        z_last = [sem(f"z_last{c}") for c in range(CH)]
        l1a_done = sem("l1a_done")
        l1b_done = sem("l1b_done")
        h1_act = sem("h1_act")
        h1_dve = sem("h1_dve")
        l2a_done = sem("l2a_done")
        l2b_done = sem("l2b_done")
        h2_act = sem("h2_act")
        h2_dve = sem("h2_dve")
        l3_done = sem("l3_done")
        y_ready = sem("y_ready")
        stored = sem("stored")
        NW = CH + 5

        block = ctx.enter_context(nc.Block())

        def pair_rows(eng, t, chunks, done):
            eng.wait_ge(g_act, copies(0, t, GSTEPS - 1))
            if gram_quadrants(t)[1]:
                eng.wait_ge(g_dve, copies(1, t, GSTEPS - 1))
            for c in chunks:
                m0, w, n0 = CHUNKS[c]
                eng.dma_start(Z[0:PAIRS[c], c, t * P:(t + 1) * P], G[n0:NF, t % 2, m0:m0 + w, :]).then_inc(done[c], 16)

        @block.gpsimd
        def _(pool):
            nc.gpsimd.iota(rown[:, :], pattern=[[1, OQ]], base=0, channel_multiplier=OQ,
                           allow_small_or_imprecise_dtypes=True).then_inc(rown_set, 1)
            nc.gpsimd.memset(eT[:, :, :, NF:FP], 0.0).then_inc(pads_set, 1)
            pool.wait_ge(ids_in, 16)
            for t in range(TILES):
                for k, (g0, n) in enumerate(TGROUPS):
                    if (t - 2, k) in TURNS:
                        pool.wait_ge(transposed, TURNS.index((t - 2, k)) + 1)
                    elif (t - 2, k) in FLIPS:
                        pool.wait_ge(flipped, NBLOCK * NBLOCK * (FLIPS.index((t - 2, k)) + 1))
                    for g in range(g0, g0 + n):
                        f = GATHER[g]
                        pool.indirect_dma_start(
                            out=E[:, t % 2, g, :], out_offset=None, in_=tables[f],
                            in_offset=bass.IndirectOffsetOnAxis(ap=ids_sb[:, t, f:f + 1], axis=0),
                        ).then_inc(rows_in[t % 2][k], 16)
            pair_rows(pool, TILES - 1, [CH - 1], z_last)

        @block.sync
        def _(sp):
            for j, f in enumerate(ONEHOT):
                a = j % 2
                if j >= 2:
                    sp.wait_ge(lo_ready, j - 1)
                    sp.wait_ge(pick_ready, (OQ - 1) * (j - 1))
                    sp.wait_ge(pick_act, j - 1)
                sp.dma_start(idb[:, a, :], ids_T[f:f + 1, :].to_broadcast([OP, B])).then_inc(idb_in[a], 16)
                if j == 0:
                    sp.dma_start(ids_sb[:, :, :], ids.rearrange("(t p) f -> p t f", p=P)).then_inc(ids_in, 16)
                table = tables[f].rearrange("(p q) d -> p (q d)", q=OQ)
                if j == 0:
                    sp.dma_start(raw[:, a, 0:HALF], table[:, 0:HALF]).then_inc(raw0_in, 16)
                    sp.dma_start(raw[:, a, HALF:], table[:, HALF:]).then_inc(raw_in[a], 16)
                else:
                    sp.dma_start(raw[:, a, :], table).then_inc(raw_in[a], 16)
                if j == 1:
                    sp.dma_start(ident[:, :], ident_d).then_inc(ident_in, 16)
            sp.wait_ge(gram_done, 1)
            for c in range(CH):
                sp.dma_start(w1[0:CROWS[c], c, :], W1[c * P:c * P + CROWS[c], :]).then_inc(w_in, 16)
            sp.dma_start(w2[:, :, :], W2.rearrange("(c p) n -> p c n", p=P)).then_inc(w_in, 16)
            sp.dma_start(w3[:, :], W3).then_inc(w_in, 16)
            sp.dma_start(b1s[:, :], b1).then_inc(w_in, 16)
            sp.dma_start(b2s[:, :], b2).then_inc(w_in, 16)
            sp.dma_start(Z[PAIRS[0]:CROWS[0], 0, :], dense_T).then_inc(w_in, 16)
            for t in range(TILES - 1):
                pair_rows(sp, t, range(CH), [z_in[t]] * CH)
            pair_rows(sp, TILES - 1, range(CH - 1), z_last)
            sp.wait_ge(y_ready, TILES)
            sp.dma_start(out, y[0:1, :]).then_inc(stored, 16)
            sp.wait_ge(stored, 16)

        @block.tensor
        def _(pe):
            pe.wait_ge(zeros_set, 1)
            for _ in range(WARMUP):
                nc.tensor.matmul(psB[:, :], zeros[:, 0:P], zeros[:, :], start=True, stop=True)

            def pick_field(j):
                if j >= 4:
                    pe.wait_ge(picked_out, j - 3)
                if j == 0:
                    pe.wait_ge(hi0_ready, 1)
                else:
                    pe.wait_ge(hi_ready, j + 1)
                first, second = range(OQ // 2), range(OQ // 2, OQ)
                if j == 0:
                    steps = [(hi, q) for q in first] + [(lo, q) for q in first]
                    steps += [(half, q) for q in second for half in (hi, lo)]
                else:
                    steps = [(half, q) for half in (hi, lo) for q in range(OQ)]
                for n, (half, q) in enumerate(steps):
                    if half is lo and q == 0:
                        pe.wait_ge(lo_ready, j + 1)
                    if half is hi and q < OQ - 1:
                        pe.wait_ge(pick_ready, (OQ - 1) * j + q + 1)
                    if half is hi and q == OQ - 1:
                        pe.wait_ge(pick_act, j + 1)
                    last = nc.tensor.matmul(psO[j % 4], half[:, j % 2, q * D:(q + 1) * D],
                                            pick[:, j % 2, q, :], start=(n == 0), stop=(n == len(steps) - 1))
                last.then_inc(picked, 1)

            def turn(t, k):
                g0, n = TGROUPS[k]
                i = TURNS.index((t, k))
                if i == 0:
                    pe.wait_ge(ident_in, 16)
                pe.wait_ge(rows_in[t % 2][k], 16 * n * (t // 2 + 1))
                if i >= 2:
                    pe.wait_ge(eT_act, i - 1)
                for g in range(n):
                    last = nc.tensor.transpose(psT[i % 2][:, g, :], E[:, t % 2, g0 + g, :], ident[:, :])
                last.then_inc(transposed, 1)

            def gram(t, s):
                i = GSTEPS * t + s
                if i == 0:
                    pe.wait_ge(pads_set, 1)
                    pe.wait_ge(picked_out, NOH)
                if s == 0:
                    pe.wait_ge(eT_act, sum(u <= t for u, _ in TURNS))
                    if t >= FLIPS[0][0]:
                        pe.wait_ge(flipped, NBLOCK * NBLOCK * sum(u <= t for u, _ in FLIPS))
                if i >= 2:
                    before = divmod(i - 2, GSTEPS)
                    pe.wait_ge(g_act, copies(0, *before))
                    if gram_quadrants(before[0])[1]:
                        pe.wait_ge(g_dve, copies(1, *before))
                for bk in range(GPAIR):
                    for r in range(NGB):
                        b0 = SSTEP * s + SG * (NGB * bk + r)
                        last = nc.tensor.matmul(
                            psG[i % 2][0:GC, bk, r * SG * NM:(r + 1) * SG * NM],
                            eT[:, t, b0:b0 + SG, :].rearrange("p s f -> p (s f)")[:, 0:GC],
                            eT[:, t, b0:b0 + SG, 0:NM], start=True, stop=True)
                last.then_inc(gram_done, 1)

            def layer1(t):
                if t == 0:
                    pe.wait_ge(w_in, NW * 16)
                elif t < TILES - 1:
                    pe.wait_ge(y_ready, t)
                blocks, _, _ = layer_psum(t)
                if t < TILES - 1:
                    pe.wait_ge(z_in[t], 16 * CH)
                    steps = [(h, c) for h in range(C1) for c in range(CH)]
                else:
                    steps = [(h, c) for c in range(CH) for h in range(C1)]
                for h, c in steps:
                    if t == TILES - 1 and h == 0:
                        pe.wait_ge(z_last[c], 16)
                    last = nc.tensor.matmul(blocks[h], w1[0:CROWS[c], c, h * P:(h + 1) * P],
                                            Z[0:CROWS[c], c, t * P:(t + 1) * P],
                                            start=(c == 0), stop=(c == CH - 1))
                    if c == CH - 1 and h % (C1 // 2) == C1 // 2 - 1:
                        last.then_inc((l1a_done, l1b_done)[h // (C1 // 2)], 1)

            def layer2(t):
                _, blocks, _ = layer_psum(t)
                for h, done in enumerate((l2a_done, l2b_done)):
                    for c in range(C1):
                        if h == 0 and c == 0:
                            pe.wait_ge(h1_act, C1 // 2 * (t + 1))
                        if h == 0 and c == C1 // 2:
                            pe.wait_ge(h1_dve, C1 // 2 * (t + 1))
                        last = nc.tensor.matmul(blocks[h], w2[:, c, h * P:(h + 1) * P], h1[:, t % 2, c, :],
                                                start=(c == 0), stop=(c == C1 - 1))
                    last.then_inc(done, 1)

            def layer3(t):
                _, _, outputs = layer_psum(t)
                for c, ready in ((0, h2_act), (1, h2_dve)):
                    pe.wait_ge(ready, t + 1)
                    last = nc.tensor.matmul(outputs, w3[:, c:c + 1], h2[:, t % 2, c, :],
                                            start=(c == 0), stop=(c == C2 - 1))
                last.then_inc(l3_done, 1)

            for kind, x, i in ORDER:
                if kind == "onehot":
                    pick_field(x)
                elif kind == "turn":
                    turn(x, i)
                elif kind == "gram":
                    gram(x, i)
                elif kind == "layer1":
                    layer1(x)
                elif kind == "layer2":
                    layer2(x)
                elif kind == "layer3":
                    layer3(x)

        def gram_out(eng, copy, t, s, samples, done):
            i = GSTEPS * t + s
            if s == 0 and t >= 2:
                eng.wait_ge(z_in[t - 2], 16 * CH)
            eng.wait_ge(gram_done, i + 1)
            for q in samples:
                src = psG[i % 2][FP * q:FP * q + NF, :, 0:NGB * SG * NM].rearrange(
                    "p k (r s m) -> p k r s m", r=NGB, s=SG)[:, :, :, q, :]
                dst = G[:, t % 2, :, SSTEP * s:SSTEP * (s + 1)].rearrange(
                    "p m (k r s) -> p k r s m", k=GPAIR, r=NGB)[:, :, :, q, :]
                copy(dst, src).then_inc(done, 1)

        @block.scalar
        def _(act):
            def last_one_hot(j):
                if j == 0:
                    act.wait_ge(rown_set, 1)
                else:
                    act.wait_ge(pick_act, j)
                act.wait_ge(idb_in[j % 2], 16 * (j // 2 + 1))
                nc.scalar.activation(dist[:, :], idb[:, j % 2, :], ACT.Abs, scale=-1.0,
                                     bias=rown[:, OQ - 1:OQ]).then_inc(dist_ready, 1)
                act.wait_ge(dist_ready, j + 1)
                if j >= 2:
                    act.wait_ge(picked, j - 1)
                nc.scalar.activation(pick[:, j % 2, OQ - 1, :], dist[:, :], ACT.Relu, scale=-1.0,
                                     bias=1.0).then_inc(pick_act, 1)

            def split_hi(j):
                if j == 0:
                    act.wait_ge(raw0_in, 16)
                    nc.scalar.copy(hi[:, 0, 0:HALF], raw[:, 0, 0:HALF]).then_inc(hi0_ready, 1)
                    act.wait_ge(raw_in[0], 16)
                    nc.scalar.copy(hi[:, 0, HALF:], raw[:, 0, HALF:]).then_inc(hi_ready, 1)
                else:
                    act.wait_ge(raw_in[j % 2], 16 * (j // 2 + 1))
                    if j >= 2:
                        act.wait_ge(picked, j - 1)
                    nc.scalar.copy(hi[:, j % 2, :], raw[:, j % 2, :]).then_inc(hi_ready, 1)

            for j in range(2):
                split_hi(j)
                last_one_hot(j)
            for kind, x, i in ORDER:
                if kind == "onehot":
                    act.wait_ge(picked, x + 1)
                    nc.scalar.copy(eT[:, :, :, x], psO[x % 4].rearrange("p (t b) -> p t b", b=P)).then_inc(picked_out, 1)
                    if x + 2 < NOH:
                        split_hi(x + 2)
                        last_one_hot(x + 2)
                elif kind == "turn":
                    g0, n = TGROUPS[i]
                    turn = TURNS.index((x, i))
                    act.wait_ge(transposed, turn + 1)
                    nc.scalar.copy(eT[:, x, :, NOH + g0:NOH + g0 + n].rearrange("p b f -> p f b"),
                                   psT[turn % 2][:, 0:n, :]).then_inc(eT_act, 1)
                elif kind == "gram":
                    gram_out(act, nc.scalar.copy, x, i, gram_quadrants(x)[0], g_act)
                elif kind == "layer1":
                    act.wait_ge(l1a_done, x + 1)
                    if x == 0:
                        act.wait_ge(w_in, NW * 16)
                    for c in range(C1 // 2):
                        nc.scalar.activation(h1[:, x % 2, c, :], layer_psum(x)[0][c], ACT.Relu,
                                             bias=b1s[:, c:c + 1]).then_inc(h1_act, 1)
                elif kind == "layer2":
                    act.wait_ge(l2a_done, x + 1)
                    nc.scalar.activation(h2[:, x % 2, 0, :], layer_psum(x)[1][0], ACT.Relu,
                                         bias=b2s[:, 0:1]).then_inc(h2_act, 1)
                elif kind == "layer3":
                    act.wait_ge(l3_done, x + 1)
                    nc.scalar.copy(y[0:1, x * P:(x + 1) * P], layer_psum(x)[2]).then_inc(y_ready, 1)

        @block.vector
        def _(dve):
            def make_pick(j):
                if j == 0:
                    dve.wait_ge(rown_set, 1)
                dve.wait_ge(idb_in[j % 2], 16 * (j // 2 + 1))
                if j >= 2:
                    dve.wait_ge(picked, j - 1)
                before = OQ // 2 if j == 0 else OQ - 1
                one_hot(j, range(before))
                dve.wait_ge(hi_ready, j + 1)
                dve.wait_ge(raw_in[j % 2], 16 * (j // 2 + 1))
                nc.vector.tensor_tensor(lo[:, j % 2, :], raw[:, j % 2, :], hi[:, j % 2, :].bitcast(F32),
                                        ALU.subtract).then_inc(lo_ready, 1)
                one_hot(j, range(before, OQ - 1))

            def one_hot(j, blocks):
                for q in blocks:
                    nc.vector.tensor_scalar(pick[:, j % 2, q, :], idb[:, j % 2, :], rown[:, q:q + 1], None,
                                            ALU.is_equal).then_inc(pick_ready, 1)

            def flip(t, k, half):
                g0, n = TGROUPS[k]
                if half == 0:
                    dve.wait_ge(rows_in[t % 2][k], 16 * n * (t // 2 + 1))
                for b0 in range(half * P // 2, (half + 1) * P // 2, BLOCK):
                    for d0 in range(0, D, BLOCK):
                        nc.vector.transpose(
                            eT[d0:d0 + BLOCK, t, b0:b0 + BLOCK, NOH + g0:NOH + g0 + n].rearrange("p b f -> p f b"),
                            E[b0:b0 + BLOCK, t % 2, g0:g0 + n, d0:d0 + BLOCK]).then_inc(flipped, 1)

            nc.vector.memset(zeros[:, :], 0.0).then_inc(zeros_set, 1)
            make_pick(0)
            make_pick(1)
            for kind, x, i in ORDER:
                if kind == "onehot":
                    if x + 2 < NOH:
                        make_pick(x + 2)
                elif kind == "flip":
                    flip(x, *i)
                elif kind == "gram":
                    if gram_quadrants(x)[1]:
                        gram_out(dve, nc.vector.tensor_copy, x, i, gram_quadrants(x)[1], g_dve)
                elif kind == "layer1":
                    dve.wait_ge(l1b_done, x + 1)
                    if x == 0:
                        dve.wait_ge(w_in, NW * 16)
                    for c in range(C1 // 2, C1):
                        nc.vector.tensor_scalar(h1[:, x % 2, c, :], layer_psum(x)[0][c], b1s[:, c:c + 1], 0.0,
                                                ALU.add, ALU.max).then_inc(h1_dve, 1)
                elif kind == "layer2":
                    dve.wait_ge(l2b_done, x + 1)
                    nc.vector.tensor_scalar(h2[:, x % 2, 1, :], layer_psum(x)[1][1], b2s[:, 1:2], 0.0,
                                            ALU.add, ALU.max).then_inc(h2_dve, 1)


def kernel(**inputs):
    import concourse.bacc as bacc
    from concourse.bass_utils import run_bass_kernel_spmd

    nc = bacc.Bacc("TRN2", target_bir_lowering=False, num_devices=1)
    arrays = {}

    def dram(name, a):
        a = np.ascontiguousarray(a)
        arrays["in_" + name] = a
        return nc.dram_tensor("in_" + name, a.shape, mybir.dt.from_np(a.dtype), kind="ExternalInput").ap()

    dense_T = dram("dense_T", np.asarray(inputs["dense_ctx"]).T)
    ids = dram("ids", np.asarray(inputs["ids"]).view(np.uint32))
    ids_T = dram("ids_T", np.asarray(inputs["ids"]).T)
    tables = [dram(f"tbl_{f}", inputs[f"tbl_{f}"]) for f in range(NF)]
    rows = w1_rows().reshape(-1)
    w1 = np.zeros((CH * P, H1), np.float32)
    w1[rows >= 0] = np.asarray(inputs["W_top1"])[rows[rows >= 0]]
    W1 = dram("W1", w1)
    b1 = dram("b1", np.asarray(inputs["b_top1"]).reshape(C1, P).T)
    W2 = dram("W2", inputs["W_top2"])
    b2 = dram("b2", np.asarray(inputs["b_top2"]).reshape(C2, P).T)
    W3 = dram("W3", np.asarray(inputs["W_top3"]).reshape(C2, P).T)
    ident = dram("ident", np.eye(P, dtype=np.float32))
    out = nc.dram_tensor("out", (B, 1), F32, kind="ExternalOutput").ap()
    build(nc, dense_T, ids, ids_T, tables, W1, b1, W2, b2, W3, ident, out.rearrange("b o -> o b"))
    r = run_bass_kernel_spmd(nc, [arrays], core_ids=[0])
    return r.results[0]["out"]
```
